# Optimizing a Trainium2 kernel written in Bass

```python
import numpy as np
import jax
import jax.numpy as jnp

def _softmax(x, axis=-1):
    return jax.nn.softmax(x, axis=axis)

def _gelu(x):
    return jax.nn.gelu(x, approximate=True)

def _silu(x):
    return jax.nn.silu(x)

def _sigmoid(x):
    return jax.nn.sigmoid(x)

def _layernorm(x, axis=-1, eps=1e-05):
    m = jnp.mean(x, axis=axis, keepdims=True)
    v = jnp.var(x, axis=axis, keepdims=True)
    return (x - m) / jnp.sqrt(v + eps)

def _scatter_add(tgt, idx, src, axis=0):
    return tgt.at[idx].add(src)

def _segment_sum(src, seg, n):
    return jax.ops.segment_sum(src, seg, n)
kernel_name = 'mk_flamingo_gated_d1_seqx_r2_b094e6'

def setup_inputs(seed: int=0):
    np.random.seed(seed)
    _w = jnp.asarray

    def _rec_inputs():
        import jax
        import jax.numpy as jnp
        _rk = jax.random.key(seed)
        x = -0.000125 + 0.9999 * jax.random.normal(jax.random.fold_in(_rk, 1), (2, 1024, 2048), jnp.float32)
        _lenS = 1024 - jax.random.randint(jax.random.fold_in(_rk, 7), (2,), 0, max(1, 1024 // 4) + 1, jnp.int32)
        _lenS2 = 2048 - jax.random.randint(jax.random.fold_in(_rk, 8), (2,), 0, max(1, 2048 // 4) + 1, jnp.int32)
        _ctx_4096P = jax.random.normal(jax.random.fold_in(_rk, 11), (2, 16, 2048), jnp.float32)
        _ctx_4096c = jax.random.dirichlet(jax.random.fold_in(_rk, 511), 0.3 * jnp.ones((16,), jnp.float32), (2, 2048))
        _ctx_4096t = jnp.einsum('bsk,bkd->bsd', _ctx_4096c, _ctx_4096P)
        _ctx_4096t = _ctx_4096t * jax.lax.rsqrt(jnp.mean(jnp.square(_ctx_4096t)) + 1e-12) * 0.953939
        ctx_4096 = -5.72187e-05 + 0.999849 * (_ctx_4096t + 0.3 * jax.random.normal(jax.random.fold_in(_rk, 611), (2, 2048, 2048), jnp.float32))
        _g = jax.random.normal(jax.random.fold_in(_rk, 9001), (2, 1), jnp.float32)
        _g = jnp.sign(_g) * jnp.maximum(jnp.abs(_g), 1.0) + (_g == 0) * 1.0
        g_xattn = _g[0]
        g_ffn = _g[1]
        return (x, ctx_4096, g_xattn, g_ffn)
    x, ctx_4096, g_xattn, g_ffn = _rec_inputs()

    def _L0_xattn_setup():
        import jax, jax.numpy as jnp
        import numpy as np
        QMIN = 0.0
        QMAX = 255.0

        def fake_quant(x, scale, zp):
            s = scale.reshape(())
            z = zp.reshape(())
            q = jnp.clip(jnp.round(x / s + z), QMIN, QMAX)
            return (q - z) * s
        key = jax.random.key(seed)
        k1, k2 = jax.random.split(key)
        B, M, K, N = (4, 1024, 2048, 2048)
        x1 = jax.random.normal(k1, (B, M, K), dtype=jnp.float32)
        x2 = jax.random.normal(k2, (B, K, N), dtype=jnp.float32)
        x1_scale = jnp.full((1,), 8.0 / 255.0, dtype=jnp.float32)
        x1_zp = jnp.full((1,), 128.0, dtype=jnp.float32)
        x2_scale = jnp.full((1,), 8.0 / 255.0, dtype=jnp.float32)
        x2_zp = jnp.full((1,), 128.0, dtype=jnp.float32)
        return {'x1': x1, 'x2': x2, 'x1_scale': x1_scale, 'x1_zp': x1_zp, 'x2_scale': x2_scale, 'x2_zp': x2_zp}
    _L0_xattn_all = _L0_xattn_setup()
    _L0_xattn_in = {k: v for k, v in _L0_xattn_all.items() if k in ('x1_scale', 'x1_zp', 'x2_scale', 'x2_zp')}
    del _L0_xattn_all

    def _L0_ffn_setup():
        import jax, jax.numpy as jnp
        import numpy as np
        NUM_EXPERTS = 4
        HIDDEN = 2048
        RANK = 8
        ALPHA = 8.0
        SCALE = ALPHA / RANK
        key = jax.random.key(seed)
        ks = jax.random.split(key, 6)
        B, T, H, E, R = (4, 2048, HIDDEN, NUM_EXPERTS, RANK)
        x = jax.random.normal(ks[0], (B, T, H), dtype=jnp.float32)
        W_up = jax.random.normal(ks[1], (H, H), dtype=jnp.float32) / np.sqrt(H)
        gate_w = jax.random.normal(ks[2], (E, H), dtype=jnp.float32) / np.sqrt(H)
        expert_bias = jnp.zeros((E,), dtype=jnp.float32)
        lora_A = jax.random.normal(ks[3], (E, R, H), dtype=jnp.float32) / np.sqrt(H)
        lora_B = jax.random.normal(ks[4], (E, H, R), dtype=jnp.float32) * 0.01
        return {'x': x, 'W_up': W_up, 'gate_w': gate_w, 'expert_bias': expert_bias, 'lora_A': lora_A, 'lora_B': lora_B}
    _L0_ffn_all = _L0_ffn_setup()
    _L0_ffn_in = {k: v for k, v in _L0_ffn_all.items() if k in ('W_up', 'gate_w', 'expert_bias', 'lora_A', 'lora_B')}
    del _L0_ffn_all
    return {'x': x, 'ctx_4096': ctx_4096, 'g_xattn': g_xattn, 'g_ffn': g_ffn, 'L0_xattn_x1_scale': _L0_xattn_in['x1_scale'], 'L0_xattn_x1_zp': _L0_xattn_in['x1_zp'], 'L0_xattn_x2_scale': _L0_xattn_in['x2_scale'], 'L0_xattn_x2_zp': _L0_xattn_in['x2_zp'], 'L0_ffn_W_up': _L0_ffn_in['W_up'], 'L0_ffn_gate_w': _L0_ffn_in['gate_w'], 'L0_ffn_expert_bias': _L0_ffn_in['expert_bias'], 'L0_ffn_lora_A': _L0_ffn_in['lora_A'], 'L0_ffn_lora_B': _L0_ffn_in['lora_B']}

def reference(x, ctx_4096, g_xattn, g_ffn, L0_xattn_x1_scale, L0_xattn_x1_zp, L0_xattn_x2_scale, L0_xattn_x2_zp, L0_ffn_W_up, L0_ffn_gate_w, L0_ffn_expert_bias, L0_ffn_lora_A, L0_ffn_lora_B):
    import jax
    import jax.numpy as jnp

    def _L0_xattn_ref(x1, x2, x1_scale, x1_zp, x2_scale, x2_zp):
        import jax, jax.numpy as jnp
        import numpy as np
        QMIN = 0.0
        QMAX = 255.0

        def fake_quant(x, scale, zp):
            s = scale.reshape(())
            z = zp.reshape(())
            q = jnp.clip(jnp.round(x / s + z), QMIN, QMAX)
            return (q - z) * s
        q1 = fake_quant(x1, x1_scale, x1_zp)
        q2 = fake_quant(x2, x2_scale, x2_zp)
        return jnp.matmul(q1, q2)

    def _L0_ffn_ref(x, W_up, gate_w, expert_bias, lora_A, lora_B):
        import jax, jax.numpy as jnp
        import numpy as np
        NUM_EXPERTS = 4
        HIDDEN = 2048
        RANK = 8
        ALPHA = 8.0
        SCALE = ALPHA / RANK
        B, T, H = x.shape
        E = gate_w.shape[0]
        x_flat = x.reshape(-1, H)
        logits = x_flat @ gate_w.T + expert_bias
        top1 = jnp.argmax(logits, axis=-1)
        one_hot = jax.nn.one_hot(top1, E, dtype=x_flat.dtype)
        base_out = jnp.einsum('bth,oh->bto', x, W_up)
        z = jnp.einsum('nh,erh->ner', x_flat, lora_A)
        d = jnp.einsum('ner,ehr->neh', z, lora_B) * SCALE
        delta = jnp.einsum('neh,ne->nh', d, one_hot)
        return base_out + delta.reshape(B, T, H)
    x = x + jnp.tanh(g_xattn[0]) * _L0_xattn_ref(_layernorm(x, axis=-1), ctx_4096, L0_xattn_x1_scale, L0_xattn_x1_zp, L0_xattn_x2_scale, L0_xattn_x2_zp)
    x = x + jnp.tanh(g_ffn[0]) * _L0_ffn_ref(_layernorm(x, axis=-1), L0_ffn_W_up, L0_ffn_gate_w, L0_ffn_expert_bias, L0_ffn_lora_A, L0_ffn_lora_B)
    return x

_drawn_inputs = setup_inputs


def setup_inputs(seed=0):
    import zlib

    import numpy as np

    out = dict(_drawn_inputs(seed))
    spreads = {'L0_ffn_expert_bias': (0.0, 0.8)}
    factors = {'L0_ffn_gate_w': 8.0, 'L0_ffn_lora_A': 8.0, 'L0_ffn_lora_B': 8.0}
    for name, (base, spread) in spreads.items():
        noise = np.random.default_rng([zlib.crc32(name.encode()), seed]).standard_normal(out[name].shape)
        drawn = base * np.exp(spread * noise) if base else spread * noise
        out[name] = jnp.asarray(drawn.astype(out[name].dtype))
    for name, factor in factors.items():
        out[name] = (out[name] * factor).astype(out[name].dtype)
    return out
```

```python
import concourse.bass as bass
from concourse import mybir
from contextlib import ExitStack

F32, BF16, F16, I32 = mybir.dt.float32, mybir.dt.bfloat16, mybir.dt.float16, mybir.dt.int32
ALU = mybir.AluOpType
ACT = mybir.ActivationFunctionType
AX = mybir.AxisListType

P = 128
MAGIC = float(2 ** 23)
EPS = 1e-5


def build(nc, x, ctx, w, b_t, scal, out):
    ROWS, D = x.shape
    TILES = ROWS // P
    KT = D // P
    PER = TILES // 2
    NB = 512
    NCH = D // NB
    E, R = 4, 8
    EXT = E + E * R
    WC = D + EXT
    CUT = [0, 416, 832, 1248, 1666, WC]
    GROUP = 8
    XB = 3
    FIRST_SUM = 7
    YS = 2.0 ** 9
    WS = 2.0 ** 14
    UN = 1.0 / (YS * WS)

    x_t = x.rearrange("(t p) d -> t p d", p=P)
    c_t = ctx.rearrange("(n p) d -> n p d", p=P)
    w_t = w.rearrange("(n p) d -> n p d", p=P)
    o_t = out.rearrange("(t p) d -> t p d", p=P)
    NCTX = c_t.shape[0]
    h_t = nc.dram_tensor("h_scratch", (TILES, P, D), F32).ap()
    bst_d = nc.dram_tensor("b_stack_scratch", (P, 2 * D), BF16).ap()

    es = ExitStack()
    with es:
        def sb(name, shape, dt):
            return es.enter_context(nc.sbuf_tensor(name, shape, dt))

        def sem(name):
            return es.enter_context(nc.semaphore(name))

        ARENA = 2 * KT * WC
        SHIFT = ARENA - NCTX * D
        arena = sb("arena", [P, ARENA], F16)
        X = sb("rows", [P, XB, D], F32)
        T = sb("normed", [P, D], F32)
        HL = sb("halves", [P, 2, D], F16)
        YT = sb("rows_T", [P, 2, KT, 2, P], F16)
        S0 = sb("stage0", [P, WC], F32)
        S1 = sb("stage1", [P, WC], F32)
        q1 = HL[:, 0, :].bitcast(BF16)
        q1T = YT[:, 1].rearrange("p k h m -> p (k h m)").bitcast(BF16).rearrange(
            "p (b k m) -> p b k m", b=2, k=KT)
        S2 = YT[:, 0].rearrange("p k h m -> p (k h m)").bitcast(F32)
        stages = [S0[:, 0:D], S1[:, 0:D], S2]
        Bst = S1[:, :].bitcast(BF16)[:, 0:2 * D].rearrange("p (j n) -> p j n", j=2)
        arena_bf = arena[:, :].bitcast(BF16)

        def Q(n):
            if isinstance(n, int):
                return arena_bf[:, SHIFT + n * D:SHIFT + (n + 1) * D]
            return arena_bf[:, bass.ds(n * D + SHIFT, D)]

        def W(kt, half, a=0, b=WC):
            if isinstance(kt, int):
                return arena[:, (2 * kt + half) * WC + a:(2 * kt + half) * WC + b]
            return arena[:, bass.ds((kt * 2 + half) * WC + a, b - a)]

        tb = arena[:, ARENA - 12 * D // 1 // 2 * 2:].rearrange("p (a n) -> p a n", n=D)
        braw = arena[:, ARENA - 2 * D:].bitcast(F32)
        bres = arena[:, ARENA - 4 * D:ARENA - 2 * D].bitcast(F32)
        bA = arena_bf[:, ARENA - 6 * D:ARENA - 5 * D]
        bB = arena_bf[:, ARENA - 5 * D:ARENA - 4 * D]

        NS = 10
        sc = sb("scal", [P, NS], F32)
        dv = sb("derived", [P, 24], F32)
        idb = sb("ident_bf", [P, P], BF16)
        idh = sb("ident_h", [P, P], F16)
        d1 = sb("delta1_parts", [P, 3, P], BF16)
        bn = sb("bn", [P, 4, 6], F32)
        ln = sb("ln", [P, 12], F32)
        rsum = sb("rsum", [P, 2], F32)
        wsum = sb("wsum", [P, KT], F32)
        wp = sb("wpow", [P, KT], F32)
        wa = sb("wscale", [P, KT], F32)
        wc = sb("wback", [P, KT], F32)
        rt = sb("route", [P, 3, E], F32)
        prio = sb("prio", [P, E], F32)
        rm = sb("route_max", [P, 2], F32)
        z = sb("z", [P, 3, E * R], F32)
        zb = sb("z_stack", [P, 2, 4, E * R], BF16)
        zT = sb("z_stack_T", [P, 2, P], BF16)

        names = ("rs1 rs2 c1 c2 m1 m2 dl1 dl2 tx tf coef cd ce pm PM rPM sc2 gs dh dm ct ctb").split()
        V = {n: dv[:, i:i + 1] for i, n in enumerate(names)}
        s1, z1, s2, z2, gx, gf = (sc[:, i:i + 1] for i in range(6))
        bias_row = sc[:, 6:6 + E]
        mean, var = ln[:, 0:1], ln[:, 1:2]
        ve, sd, u, au, bu, rstd, nmr = (ln[:, i:i + 1] for i in range(2, 9))

        bank = [es.enter_context(nc.psum_tensor(f"bank{i}", [P, NB], F32)) for i in range(8)]
        TR = [bank[5][:, :], bank[6][:, :]]
        ZP = bank[7][:, 0:P].bitcast(BF16)
        ztr = ZP.rearrange("p (j m) -> p j m", j=2)

        s_scal = sem("scal_loaded"); s_braw = sem("b_loaded"); s_bst = sem("b_stack_parked")
        s_bback = sem("b_stack_loaded")
        s_x = sem("row_tile_loaded"); s_st = sem("row_tile_stored")
        s_c = [sem(f"ctx_loaded{i}") for i in range(3)]
        s_w0 = sem("w_loaded0"); s_w1 = sem("w_loaded1")
        s_id = sem("constants_made"); s_dv = sem("derived_step"); s_tanh = sem("tanh_done")
        s_pool = sem("pool_step")
        s_bn = sem("bn_done"); s_ag = sem("aggr_done"); s_ve = sem("var_eps"); s_sd = sem("sd_done")
        s_nt = sem("newton_step"); s_norm = sem("normed"); s_relu = sem("relu_done"); s_clip = sem("clipped")
        s_q1 = sem("q1_ready"); s_xp = sem("x_corrected"); s_rs = sem("row_term")
        s_tr = sem("transposed"); s_ev = sem("transposes_out")
        s_mm = sem("chunk_done"); s_epi = sem("chunk_out")
        s_cr = sem("ctx_relu"); s_cc = sem("ctx_clipped"); s_q2 = sem("ctx_ready")
        s_sum = sem("w_abs_sum"); s_wp = sem("w_pow"); s_wa = sem("w_scale"); s_hi = sem("w_high")
        s_lo = sem("w_ready"); s_fr = sem("ctx_tile_free")
        s_pm = sem("pow_max"); s_PM = sem("pow_max_all"); s_sc = sem("scales_ready")
        s_yh = sem("y_high"); s_yl = sem("y_low"); s_yt = sem("yT_group"); s_ye = sem("yT_out")
        s_m2 = sem("chunk2_done"); s_dl = sem("delta_done"); s_rt = sem("route_step"); s_zs = sem("z_stack_ready")
        s_zt = sem("z_transposed"); s_ze = sem("zT_ready"); s_e2 = sem("chunk2_out")

        block = es.enter_context(nc.Block())

        def Xt(t):
            return X[:, t % XB, :]

        def Xc(t, a, b):
            if isinstance(t, int):
                return X[:, t % XB, a:b]
            return X[:, t % XB, a:b]

        @block.sync
        def _(sp):
            def row(t, src):
                if not isinstance(t, int) or t >= XB:
                    sp.wait_ge(s_st, 16 * (t - XB + 1))
                if not isinstance(t, int) or t >= 1:
                    sp.wait_ge(s_x, 16 * t)
                sp.dma_start(Xt(t), src).then_inc(s_x, 16)

            def ctx_tile(n, i):
                if not isinstance(n, int) or n >= 3:
                    sp.wait_ge(s_q2, n - 2)
                sp.dma_start(stages[i], c_t[n]).then_inc(s_c[i], 16)

            def load_w(buf, n):
                sp.dma_start(buf[:, :], w_t[n]).then_inc(s_w0 if buf is S0 else s_w1, 16)

            sp.dma_start(sc[:, :], scal).then_inc(s_scal, 16)
            row(0, x_t[0])
            for i in range(3):
                ctx_tile(i, i)
            row(1, x_t[1])
            with sp.Fori(1, 4) as g:
                for i in range(3):
                    ctx_tile(g * 3 + i, i)
            row(2, x_t[2])
            with sp.Fori(4, 6) as g:
                for i in range(3):
                    ctx_tile(g * 3 + i, i)
            with sp.Fori(1, 5) as j:
                for i in range(3):
                    ctx_tile(j * 3 + 15 + i, i)
                row(j + 2, x_t[j + 2])
            ctx_tile(30, 0)
            ctx_tile(31, 1)
            sp.wait_ge(s_q2, 31)
            load_w(S0, FIRST_SUM)
            row(7, x_t[7])
            with sp.Fori(0, 2) as g:
                for i in range(4):
                    if i == 0:
                        sp.wait_ge(s_q2, NCTX)
                    sp.wait_ge(s_sum, 4 * g + max(i, 1))
                    load_w(S0 if i % 2 else S1, g * 4 + i + FIRST_SUM + 1)
                row(g + 8, x_t[g + 8])
            sp.wait_ge(s_sum, 8)
            load_w(S1, 0)
            row(10, x_t[10])
            with sp.Fori(1, 6) as j:
                sp.wait_ge(s_lo, j)
                load_w(S1, j)
                row(j + 10, x_t[j + 10])
            sp.wait_ge(s_lo, 6)
            load_w(S1, 6)
            row(TILES, h_t[0])
            for n in range(FIRST_SUM, KT):
                sp.wait_ge(s_sum, 9)
                if n > FIRST_SUM:
                    sp.wait_ge(s_lo, n - 1)
                load_w(S0 if n % 2 else S1, n)
                if n == FIRST_SUM:
                    row(TILES + 1, h_t[1])
            sp.wait_ge(s_lo, 15)
            sp.wait_ge(s_bst, 16)
            sp.dma_start(Bst.rearrange("p j n -> p (j n)"), bst_d).then_inc(s_bback, 16)
            with sp.Fori(2, TILES) as s:
                row(s + TILES, h_t[s])

        @block.gpsimd
        def _(pool):
            for qd in range(4):
                pool.dma_start(braw[32 * qd:32 * qd + 32, :], b_t).then_inc(s_braw, 16)
            for m in (idb, idh):
                nc.gpsimd.memset(m[:, :], 0.0).then_inc(s_pool, 1)
            for e in range(E):
                nc.gpsimd.memset(prio[:, e:e + 1], float(E - e)).then_inc(s_id, 1)
            nc.gpsimd.memset(d1[:, :, :], 0.0).then_inc(s_id, 1)
            pool.wait_ge(s_pool, 2)
            for m in (idb, idh):
                nc.gpsimd.affine_select(out=m[:, :], in_=m[:, :], compare_op=ALU.not_equal, fill=1.0, base=0,
                                        pattern=[[-1, P]], channel_multiplier=1).then_inc(s_id, 1)
            pool.wait_ge(s_braw, 64)
            nc.gpsimd.tensor_copy(bA, braw).then_inc(s_pool, 1)
            pool.wait_ge(s_pool, 3)
            nc.gpsimd.tensor_tensor(bres, braw, bA, ALU.subtract).then_inc(s_pool, 1)
            pool.wait_ge(s_pool, 4)
            nc.gpsimd.tensor_copy(bB, bres).then_inc(s_pool, 1)
            pool.wait_ge(s_pool, 5)
            nc.gpsimd.tensor_tensor(bres, bres, bB, ALU.subtract).then_inc(s_pool, 1)
            pool.wait_ge(s_pool, 6)
            nc.gpsimd.tensor_copy(bA[32:64, :], bB[32:64, :]).then_inc(s_pool, 1)
            nc.gpsimd.tensor_copy(bA[96:128, :], bB[96:128, :]).then_inc(s_pool, 1)
            nc.gpsimd.tensor_copy(bB[0:32, :], bres[0:32, :]).then_inc(s_pool, 1)
            nc.gpsimd.tensor_copy(bB[64:96, :], bres[64:96, :]).then_inc(s_pool, 1)
            pool.wait_ge(s_pool, 8)
            nc.gpsimd.tensor_copy(bB[32:64, :], braw[32:64, :]).then_inc(s_pool, 1)
            pool.wait_ge(s_pool, 11)
            pool.dma_start(bst_d[:, 0:D], bA).then_inc(s_bst, 8 * 2)
            pool.wait_ge(s_bst, 16)
            pool.dma_start(bst_d[:, D:2 * D], bB).then_inc(s_bst, 16)
            pool.wait_ge(s_pm, 1)
            nc.gpsimd.partition_all_reduce(V["PM"], V["pm"], P, bass.bass_isa.ReduceOp.max).then_inc(s_PM, 1)
            pool.wait_ge(s_bst, 32)

        @block.scalar
        def _(act):
            A = nc.scalar.activation

            def sqrt(t):
                act.wait_ge(s_ve, t + 1)
                A(sd, ve, ACT.Sqrt).then_inc(s_sd, 1)

            def relu(t):
                act.wait_ge(s_norm, t + 1)
                A(T[:, :], T[:, :], ACT.Relu, bias=z1, scale=V["rs1"]).then_inc(s_relu, 1)

            def quant(t):
                act.wait_ge(s_clip, t + 1)
                if not isinstance(t, int) or t >= 1:
                    act.wait_ge(s_tr, 2 * t)
                    act.wait_ge(s_xp, t)
                A(q1, T[:, :], ACT.Identity, bias=V["m1"], accum_out=rsum[:, 0:1]).then_inc(s_q1, 1)
                with act.If_ne(flag2, 0):
                    act.wait_ge(s_q1, t + 1)
                    A(rsum[:, 1:2], rsum[:, 0:1], ACT.Identity, bias=V["ce"], scale=V["cd"]).then_inc(s_rs, 1)
                    act.wait_ge(s_rs, t + 1)
                    A(Xt(t), Xt(t), ACT.Identity, bias=rsum[:, 1:2]).then_inc(s_xp, 1)
                with act.Else():
                    act.sem_inc(s_xp, 1)

            def store(t, dst):
                act.wait_ge(s_epi, NCH * (t + 1))
                if not isinstance(t, int) or t >= 1:
                    act.wait_ge(s_st, 16 * t)
                act.dma_start(dst, Xt(t)).then_inc(s_st, 16)

            def store2(s):
                act.wait_ge(s_e2, 5 * (s + 1))
                act.wait_ge(s_st, 16 * (s + TILES))
                act.dma_start(o_t[s], Xt(s + TILES)).then_inc(s_st, 16)

            def evac(t, g, par):
                act.wait_ge(s_tr, 2 * t + g + 1)
                if not isinstance(t, int) or t >= 2:
                    act.wait_ge(s_mm, NCH * (t - 1))
                A(q1T[:, par, GROUP * g:GROUP * (g + 1), :].rearrange("p k m -> p (k m)"),
                  TR[g].bitcast(BF16), ACT.Copy).then_inc(s_ev, 1)

            def ctx_relu(n, i, count):
                act.wait_ge(s_c[i], 16 * (count + 1))
                A(stages[i], stages[i], ACT.Relu, bias=z2, scale=V["rs2"]).then_inc(s_cr, 1)

            def abs_sum(n, buf, count, dst):
                act.wait_ge(s_w0 if buf is S0 else s_w1, 16 * count)
                A(dst, buf[:, :], ACT.Abs, accum_out=wsum[:, n:n + 1] if isinstance(n, int)
                  else wsum[:, bass.ds(n, 1)]).then_inc(s_sum, 1)

            def w_high(n, buf):
                act.wait_ge(s_wa, n + 1)
                A(W(n, 0), buf[:, :], ACT.Identity, scale=wa[:, n:n + 1] if isinstance(n, int)
                  else wa[:, bass.ds(n, 1)]).then_inc(s_hi, 1)

            def y_high(s):
                act.wait_ge(s_norm, s + TILES + 1)
                if isinstance(s, int) and s == 0:
                    act.wait_ge(s_tr, 2 * TILES)
                else:
                    act.wait_ge(s_yt, 4 * s)
                    act.wait_ge(s_yl, s)
                A(HL[:, 0, :], Xt(s + TILES), ACT.Identity, bias=nmr, scale=rstd).then_inc(s_yh, 1)

            def z_out(s):
                act.wait_ge(s_zt, s + 1)
                if not isinstance(s, int) or s >= 1:
                    act.wait_ge(s_dl, 5 * s)
                A(zT[:, :, :].rearrange("p j m -> p (j m)"), ZP, ACT.Copy).then_inc(s_ze, 1)

            act.wait_ge(s_scal, 16)
            A(V["tx"], gx, ACT.Tanh).then_inc(s_tanh, 1)
            A(V["tf"], gf, ACT.Tanh).then_inc(s_tanh, 1)
            flag2 = act.alloc_register("delta2_bits")
            act.wait_ge(s_id, 8 + E)
            act.reg_load(flag2, V["dl2"][0:1, :].bitcast(I32))

            sqrt(0); relu(0)
            ctx_relu(0, 0, 0)
            quant(0)
            for i in (1, 2):
                ctx_relu(i, i, 0)
            for g in range(2):
                evac(0, g, 0)
            with act.Fori(1, 3) as g:
                for i in range(3):
                    ctx_relu(g * 3 + i, i, g)
            sqrt(1); relu(1)
            for i in range(3):
                ctx_relu(9 + i, i, 3)
            quant(1)
            with act.Fori(4, 6) as g:
                for i in range(3):
                    ctx_relu(g * 3 + i, i, g)
            for g in range(2):
                evac(1, g, 1)

            def period(j, par, extra_early, extra_late):
                sqrt(j + 1); relu(j + 1)
                extra_early()
                quant(j + 1)
                store(j - 1, h_t[j - 1])
                extra_late()
                for g in range(2):
                    evac(j + 1, g, par)

            with act.Fori(0, 2) as i2:
                for o in range(2):
                    j = i2 * 2 + (1 + o)
                    period(j, o, lambda: ctx_relu(j * 3 + 15, 0, j + 5),
                           lambda: [ctx_relu(j * 3 + 15 + i, i, j + 5) for i in (1, 2)])
            period(5, 0, lambda: ctx_relu(30, 0, 10),
                   lambda: (ctx_relu(31, 1, 10), abs_sum(7, S0, 1, S0[:, :])))
            period(6, 1, lambda: abs_sum(8, S1, 1, S1[:, :]),
                   lambda: [abs_sum(8 + i, S0 if i % 2 else S1, (i + 1) // 2 + 1, (S0 if i % 2 else S1)[:, :]) for i in (1, 2, 3)])
            period(7, 0, lambda: abs_sum(12, S1, 3, S1[:, :]),
                   lambda: [abs_sum(12 + i, S0 if i % 2 else S1, (i + 1) // 2 + 3, (S0 if i % 2 else S1)[:, :]) for i in (1, 2, 3)])

            def slot_sum(n):
                act.wait_ge(s_mm, NCH * PER)
                abs_sum(n, S1, n + 5, arena[:, n * 2 * WC:(n + 1) * 2 * WC].bitcast(F32) if isinstance(n, int)
                        else arena[:, bass.ds(n * (2 * WC), 2 * WC)].bitcast(F32))

            with act.Fori(0, 3) as i2:
                for o in range(2):
                    n = i2 * 2 + o
                    period(n + 8, 1 - o, lambda: slot_sum(n), lambda: w_high(n, S1))
            period(14, 1, lambda: slot_sum(6), lambda: w_high(6, S1))

            def slot(n):
                buf = S0 if n % 2 else S1
                act.wait_ge(s_w0 if n % 2 else s_w1, 16 * ((n - 7) // 2 + 6) if n % 2 else 16 * ((n - 8) // 2 + 12))
                need = -(-((n + 1) * 2 * WC - SHIFT) // D) - KT
                if need >= KT:
                    act.wait_ge(s_mm, NCH * TILES)
                elif need > 0:
                    act.wait_ge(s_fr, need)
                w_high(n, buf)

            sqrt(16)
            y_high(0)
            store(14, h_t[14])
            for n in range(7, 11):
                slot(n)
            store(15, h_t[15])
            for n in range(11, KT):
                slot(n)
            sqrt(17)
            y_high(1)
            z_out(0)
            with act.Fori(1, TILES - 1) as s:
                store2(s - 1)
                z_out(s)
                sqrt(s + TILES + 1)
                y_high(s + 1)
            store2(TILES - 2)
            z_out(TILES - 1)
            store2(TILES - 1)
            act.wait_ge(s_st, 16 * 2 * TILES)

        @block.vector
        def _(dve):
            v = nc.vector
            steps = [0]

            def step(ins):
                steps[0] += 1
                ins.then_inc(s_dv, 1)
                dve.wait_ge(s_dv, steps[0])

            dve.wait_ge(s_scal, 16)
            step(v.reciprocal(V["rs1"], s1))
            step(v.reciprocal(V["rs2"], s2))
            for zz, c, m, dl in ((z1, "c1", "m1", "dl1"), (z2, "c2", "m2", "dl2")):
                step(v.tensor_scalar(V[c], zz, 0.0, 255.0, ALU.max, ALU.min))
                step(v.tensor_scalar(V[c], V[c], MAGIC, -MAGIC, ALU.add, ALU.add))
                step(v.tensor_scalar(V[m], V[c], -1.0, -MAGIC, ALU.mult, ALU.add))
                step(v.tensor_tensor(V[dl], zz, V[c], ALU.subtract))
            dve.wait_ge(s_tanh, 2)
            step(v.tensor_tensor(V["coef"], s1, s2, ALU.mult))
            step(v.tensor_tensor(V["coef"], V["coef"], V["tx"], ALU.mult))
            step(v.tensor_scalar(V["cd"], V["coef"], V["dl2"], -1.0, ALU.mult, ALU.mult))
            step(v.tensor_scalar(V["ce"], V["cd"], V["dl1"], -float(D), ALU.mult, ALU.mult))
            dve.wait_ge(s_id, 3 + E)
            step(v.tensor_scalar(V["ct"], V["dl1"], -1.0, None, ALU.mult))
            for i in range(3):
                step(v.tensor_scalar(d1[:, i, :], d1[:, i, :], V["ct"], None, ALU.add))
                if i < 2:
                    step(v.tensor_tensor(V["ct"], V["ct"], d1[:, i, 0:1], ALU.subtract))
            v.tensor_scalar(V["dh"], V["ct"], 1.0, None, ALU.mult).then_inc(s_id, 5)

            def stats(t, scaled):
                dve.wait_ge(s_x, 16 * (t + 1))
                for i in range(4):
                    v.bn_stats(bn[:, i, :], Xc(t, i * 512, (i + 1) * 512)).then_inc(s_bn, 1)
                if scaled and not (isinstance(t, int) and t == TILES):
                    dve.wait_ge(s_yh, t - TILES)
                dve.wait_ge(s_bn, 4 * (t + 1))
                v.memset(ln[:, 9:10], 0.0)
                v.bn_aggr(ln[:, 0:2], bn[:, :, :].rearrange("p a b -> p (a b)")).then_inc(s_ag, 1)
                dve.wait_ge(s_ag, t + 1)
                v.tensor_scalar(ve, var, EPS, None, ALU.add).then_inc(s_ve, 1)
                dve.wait_ge(s_sd, t + 1)
                k = 5 if scaled else 4
                base = 5 * (t - TILES) + 4 * TILES if scaled else 4 * t
                v.reciprocal(u, sd).then_inc(s_nt, 1)
                dve.wait_ge(s_nt, base + 1)
                v.scalar_tensor_tensor(out=au, in0=u, scalar=u, in1=ve, op0=ALU.mult, op1=ALU.mult).then_inc(s_nt, 1)
                dve.wait_ge(s_nt, base + 2)
                f = YS if scaled else 1.0
                v.tensor_scalar(bu, au, -0.5 * f, 1.5 * f, ALU.mult, ALU.add).then_inc(s_nt, 1)
                dve.wait_ge(s_nt, base + 3)
                v.tensor_tensor(rstd, u, bu, ALU.mult).then_inc(s_nt, 1)
                dve.wait_ge(s_nt, base + 4)
                if scaled:
                    v.scalar_tensor_tensor(out=nmr, in0=mean, scalar=-1.0, in1=rstd, op0=ALU.mult,
                                           op1=ALU.mult).then_inc(s_nt, 1)
                    dve.wait_ge(s_nt, base + 5)
                    if isinstance(t, int) and t == TILES:
                        dve.wait_ge(s_q1, TILES)
                    else:
                        dve.wait_ge(s_yl, t - TILES)
                elif not isinstance(t, int) or t >= 1:
                    dve.wait_ge(s_q1, t)
                v.tensor_scalar(T[:, :], Xt(t), mean, rstd, ALU.subtract, ALU.mult).then_inc(s_norm, 1)

            def clip(t):
                dve.wait_ge(s_relu, t + 1)
                v.tensor_scalar(T[:, :], T[:, :], 255.0, MAGIC, ALU.min, ALU.add).then_inc(s_clip, 1)

            def epi(t):
                dve.wait_ge(s_xp, t + 1)
                for n in range(NCH):
                    dve.wait_ge(s_mm, NCH * t + n + 1)
                    xs = Xc(t, n * NB, (n + 1) * NB)
                    v.scalar_tensor_tensor(out=xs, in0=bank[n][:, :], scalar=V["coef"], in1=xs,
                                           op0=ALU.mult, op1=ALU.add).then_inc(s_epi, 1)

            def ctx_quant(n, i):
                dve.wait_ge(s_cr, n + 1)
                v.tensor_scalar(stages[i], stages[i], 255.0, MAGIC, ALU.min, ALU.add).then_inc(s_cc, 1)
                dve.wait_ge(s_cc, n + 1)
                v.tensor_scalar(Q(n), stages[i], V["m2"], None, ALU.add).then_inc(s_q2, 1)

            def powers(a, b, sums, count):
                dve.wait_ge(s_sum, sums)
                pc = wp[:, a:b] if isinstance(a, int) else wp[:, bass.ds(a, 1)]
                wcol = wsum[:, a:b] if isinstance(a, int) else wsum[:, bass.ds(a, 1)]
                ac = wa[:, a:b] if isinstance(a, int) else wa[:, bass.ds(a, 1)]
                v.tensor_scalar(pc, wcol, 2.0 ** -100, 2.0 ** 126, ALU.max, ALU.min).then_inc(s_wp, 1)
                dve.wait_ge(s_wp, count * 4 + 1)
                v.tensor_scalar(pc.bitcast(I32), pc.bitcast(I32), 0x7F800000, None, ALU.bitwise_and).then_inc(s_wp, 1)
                dve.wait_ge(s_wp, count * 4 + 2)
                v.reciprocal(ac, pc).then_inc(s_wp, 1)
                dve.wait_ge(s_wp, count * 4 + 3)
                v.tensor_scalar(ac, ac, WS, None, ALU.mult).then_inc(s_wp, 1)
                dve.wait_ge(s_wp, count * 4 + 4)

            def w_low(n, buf):
                dve.wait_ge(s_hi, n + 1)
                v.scalar_tensor_tensor(out=W(n, 1), in0=buf[:, :],
                                       scalar=wa[:, n:n + 1] if isinstance(n, int) else wa[:, bass.ds(n, 1)],
                                       in1=W(n, 0), op0=ALU.mult, op1=ALU.subtract).then_inc(s_lo, 1)

            def y_low(s):
                dve.wait_ge(s_yh, s + 1)
                if not isinstance(s, int) or s >= 1:
                    dve.wait_ge(s_yt, 4 * s)
                v.tensor_tensor(HL[:, 1, :], T[:, :], HL[:, 0, :], ALU.subtract).then_inc(s_yl, 1)

            def yT_out(s, g, par):
                dve.wait_ge(s_yt, 4 * s + g + 1)
                src = TR[g % 2].bitcast(F16).rearrange("p (a m) -> p a m", a=4)
                dst = YT[:, par, 4 * g:4 * g + 4].rearrange("p k h m -> p k (h m)")
                back = wc[:, 4 * g:4 * g + 4].unsqueeze(2).to_broadcast([P, 4, 2 * P])
                v.tensor_tensor(dst, src, back, ALU.mult).then_inc(s_ye, 1)

            def route(s):
                base = 16 * s
                G = bank[0][:, 0:E]
                Z = bank[0][:, E:EXT]
                k = [0]

                def link(ins):
                    k[0] += 1
                    ins.then_inc(s_rt, 1)
                    dve.wait_ge(s_rt, base + k[0])

                dve.wait_ge(s_m2, 5 * s + 1)
                link(v.scalar_tensor_tensor(out=rt[:, 0, :], in0=G, scalar=V["sc2"], in1=bias_row,
                                            op0=ALU.mult, op1=ALU.add))
                link(v.tensor_reduce(rm[:, 0:1], rt[:, 0, :], AX.X, ALU.max))
                link(v.scalar_tensor_tensor(out=rt[:, 1, :], in0=rt[:, 0, :], scalar=rm[:, 0:1], in1=prio[:, :],
                                            op0=ALU.is_ge, op1=ALU.mult))
                link(v.tensor_reduce(rm[:, 1:2], rt[:, 1, :], AX.X, ALU.max))
                link(v.tensor_scalar(rt[:, 2, :], rt[:, 1, :], rm[:, 1:2], None, ALU.is_equal))
                z0 = z[:, 0, :]
                link(v.tensor_tensor(z0.rearrange("p (e r) -> p e r", e=E), Z.rearrange("p (e r) -> p e r", e=E),
                                     rt[:, 2, :].unsqueeze(2).to_broadcast([P, E, R]), ALU.mult))
                if not isinstance(s, int) or s >= 1:
                    dve.wait_ge(s_zt, s)
                link(v.tensor_copy(zb[:, 0, 0, :], z0))
                link(v.tensor_tensor(z[:, 1, :], z0, zb[:, 0, 0, :], ALU.subtract))
                link(v.tensor_copy(zb[:, 0, 2, :], z[:, 1, :]))
                link(v.tensor_tensor(z[:, 2, :], z[:, 1, :], zb[:, 0, 2, :], ALU.subtract))
                link(v.tensor_copy(zb[:, 0, 1, :], zb[:, 0, 0, :]))
                link(v.tensor_copy(zb[:, 0, 3, :], zb[:, 0, 2, :]))
                link(v.tensor_copy(zb[:, 1, 0, :], zb[:, 0, 0, :]))
                link(v.tensor_copy(zb[:, 1, 1, :], z[:, 2, :]))
                link(v.tensor_copy(zb[:, 1, 2, :], zb[:, 0, 2, :]))
                link(v.tensor_copy(zb[:, 1, 3, :], z[:, 2, :]))
                assert k[0] == 16
                dve.sem_inc(s_zs, 1)

            def epi2(s, c):
                a, b = max(CUT[c], EXT), CUT[c + 1]
                dve.wait_ge(s_dl, 5 * s + c + 1)
                xs = Xc(s + TILES, a - EXT, b - EXT)
                v.scalar_tensor_tensor(out=xs, in0=bank[c][:, a - CUT[c]:b - CUT[c]], scalar=V["gs"], in1=xs,
                                       op0=ALU.mult, op1=ALU.add).then_inc(s_e2, 1)

            stats(0, False)
            clip(0)
            for i in range(3):
                ctx_quant(i, i)
            with dve.Fori(1, 3) as g:
                for i in range(3):
                    ctx_quant(g * 3 + i, i)
            stats(1, False)
            for i in range(3):
                if i == 1:
                    clip(1)
                ctx_quant(9 + i, i)
            dve.wait_ge(s_bst, 32)
            with dve.Fori(4, 6) as g:
                for i in range(3):
                    ctx_quant(g * 3 + i, i)

            def period(j, extra):
                stats(j + 1, False)
                epi(j - 1)
                clip(j + 1)
                extra()

            with dve.Fori(1, 5) as j:
                period(j, lambda: [ctx_quant(j * 3 + 15 + i, i) for i in range(3)])
            period(5, lambda: [ctx_quant(30 + i, i) for i in range(2)])
            with dve.Fori(6, 8) as j:
                period(j, lambda: None)

            def slot(n):
                powers(n, None if not isinstance(n, int) else n + 1, n + 10, n + 1)
                dve.sem_inc(s_wa, 1)
                w_low(n, S1)

            powers(FIRST_SUM, KT, 9, 0)
            with dve.Fori(8, 14) as j:
                period(j, lambda: slot(j - 8))
            period(14, lambda: slot(6))
            dve.sem_inc(s_wa, KT - FIRST_SUM)
            v.tensor_reduce(V["pm"], wp[:, :], AX.X, ALU.max).then_inc(s_pm, 1)

            stats(16, True)
            epi(14)
            y_low(0)
            dve.wait_ge(s_PM, 1)
            step(v.reciprocal(V["rPM"], V["PM"]))
            step(v.tensor_scalar(wc[:, :], wp[:, :], V["rPM"], None, ALU.mult))
            step(v.tensor_scalar(V["sc2"], V["PM"], UN, None, ALU.mult))
            step(v.tensor_tensor(V["gs"], V["sc2"], V["tf"], ALU.mult))
            for g in range(4):
                if g == 2:
                    w_low(7, S0)
                yT_out(0, g, 0)
            w_low(8, S1)
            w_low(9, S0)
            epi(15)
            for n in range(10, KT):
                w_low(n, S0 if n % 2 else S1)
            stats(17, True)
            y_low(1)
            route(0)
            dve.wait_ge(s_mm, NCH * TILES)
            for g in range(4):
                yT_out(1, g, 1)
            for c in range(5):
                epi2(0, c)

            def tile2(s, par):
                route(s)
                stats(s + TILES + 1, True)
                y_low(s + 1)
                for c in range(3):
                    epi2(s, c)
                for g in range(4):
                    if g == 2:
                        epi2(s, 3)
                    yT_out(s + 1, g, par)
                epi2(s, 4)

            with dve.Fori(0, TILES // 2 - 1) as i2:
                for o in range(2):
                    tile2(i2 * 2 + (1 + o), o)
            route(TILES - 1)
            for c in range(5):
                epi2(TILES - 1, c)

        @block.tensor
        def _(pe):
            mmul = nc.tensor.matmul

            def transposes(t):
                pe.wait_ge(s_q1, t + 1)
                for g in range(2):
                    if not isinstance(t, int) or t >= 1:
                        pe.wait_ge(s_ev, 2 * t - 1 + g)
                    for i in range(GROUP):
                        k = GROUP * g + i
                        mm = nc.tensor.transpose(TR[g].bitcast(BF16)[:, i * P:(i + 1) * P],
                                                 q1[:, k * P:(k + 1) * P], idb[:, :])
                    mm.then_inc(s_tr, 1)

            def column_term(n, base):
                for i in range(3):
                    for kt in range(KT):
                        mm = mmul(bank[n][:, :], d1[:, i, :], Q(base + kt)[:, n * NB:(n + 1) * NB],
                                  start=False, stop=(i == 2 and kt == KT - 1), skip_group_check=True)
                return mm

            def free(t, n):
                if not isinstance(t, int) or t >= 1:
                    pe.wait_ge(s_epi, NCH * (t - 1) + n + 1)

            def by_chunks(t, par, base, slow, nxt):
                pe.wait_ge(s_ev, 2 * t + 2)
                for n in range(NCH):
                    free(t, n)
                    for kt in range(KT):
                        mm = mmul(bank[n][:, :], q1T[:, par, kt, :], Q(base + kt)[:, n * NB:(n + 1) * NB],
                                  start=(kt == 0), stop=(kt == KT - 1 and not slow), skip_group_check=slow)
                    if slow:
                        mm = column_term(n, base)
                    mm.then_inc(s_mm, 1)
                    if n == 2 and nxt:
                        transposes(t + 1)

            def by_depth(t, par, base, slow, at):
                pe.wait_ge(s_ev, 2 * t + 2)
                for n in range(NCH):
                    free(t, n)
                for kt in range(KT):
                    if t == 0:
                        pe.wait_ge(s_q2, kt + 1)
                    for n in range(NCH):
                        mm = mmul(bank[n][:, :], q1T[:, par, kt, :], Q(base + kt)[:, n * NB:(n + 1) * NB],
                                  start=(kt == 0), stop=(kt == KT - 1 and not slow), skip_group_check=slow)
                        if kt == KT - 1 and not slow:
                            mm.then_inc(s_mm, 1)
                    if t == TILES - 1 and not slow and kt < KT - 1:
                        freed(kt, mm)
                    at(kt)
                if slow:
                    for n in range(NCH):
                        column_term(n, base).then_inc(s_mm, 1)
                    if t == TILES - 1:
                        pe.sem_inc(s_fr, KT)

            def freed(kt, mm):
                mm.then_inc(s_fr, 1)

            def stage1(slow):
                by_depth(0, 0, 0, slow, lambda kt: transposes(1) if kt == 14 else None)
                by_chunks(1, 1, 0, slow, True)
                with pe.Fori(0, PER // 2 - 1) as i2:
                    for o in range(2):
                        by_chunks(i2 * 2 + (2 + o), o, 0, slow, True)
                pe.wait_ge(s_q2, NCTX)
                with pe.Fori(0, PER // 2 - 1) as i2:
                    for o in range(2):
                        by_chunks(i2 * 2 + (PER + o), o, KT, slow, True)
                by_chunks(TILES - 2, 0, KT, slow, True)
                by_depth(TILES - 1, 1, KT, slow,
                         lambda kt: y_transposes(0, kt // 2 - 4) if kt >= 8 and kt % 2 == 1 else None)

            def y_transposes(s, g):
                if g == 0:
                    pe.wait_ge(s_yl, s + 1)
                if isinstance(s, int) and s == 0 and g < 2:
                    pe.wait_ge(s_ev, 2 * TILES)
                else:
                    pe.wait_ge(s_ye, 4 * s + g - 1)
                for i in range(8):
                    k, h = 4 * g + i // 2, i % 2
                    mm = nc.tensor.transpose(TR[g % 2].bitcast(F16)[:, i * P:(i + 1) * P],
                                             HL[:, h, k * P:(k + 1) * P], idh[:, :])
                mm.then_inc(s_yt, 1)

            def products(c, kts, par, first, wait_w=False):
                a, b = CUT[c], CUT[c + 1]
                for kt in kts:
                    for yh, wh in ((0, 0), (0, 1), (1, 0)):
                        mm = mmul(bank[c][:, 0:b - a], YT[:, par, kt, yh, :], W(kt, wh, a, b),
                                  start=(first and kt == kts[0] and yh == 0 and wh == 0), stop=False,
                                  skip_group_check=True)
                return mm

            def lora(c):
                a, b = max(CUT[c], EXT), CUT[c + 1]
                for j in range(2):
                    mm = mmul(bank[c][:, a - CUT[c]:b - CUT[c]], zT[:, j, :], Bst[:, j, a - EXT:b - EXT],
                              start=False, stop=(j == 1), skip_group_check=True)
                mm.then_inc(s_dl, 1)

            def z_transposes(s):
                pe.wait_ge(s_zs, s + 1)
                if not isinstance(s, int) or s >= 1:
                    pe.wait_ge(s_ze, s)
                for j in range(2):
                    mm = nc.tensor.transpose(ztr[:, j, :], zb[:, j, :, :].rearrange("p a b -> p (a b)"), idb[:, :])
                mm.then_inc(s_zt, 1)

            def free2(s, c):
                pe.wait_ge(s_e2, 5 * (s - 1) + c + 1)

            def tile2(s, par, nxt):
                pe.wait_ge(s_ye, 4 * s + 4)
                for c in range(3):
                    free2(s, c)
                    products(c, range(KT), par, True).then_inc(s_m2, 1)
                    if c == 1:
                        z_transposes(s)
                pe.wait_ge(s_ze, s + 1)
                for c in range(3):
                    lora(c)
                if nxt:
                    y_transposes(s + 1, 0)
                    y_transposes(s + 1, 1)
                free2(s, 3)
                products(3, range(KT), par, True).then_inc(s_m2, 1)
                lora(3)
                if nxt:
                    y_transposes(s + 1, 2)
                    y_transposes(s + 1, 3)
                free2(s, 4)
                products(4, range(KT), par, True).then_inc(s_m2, 1)
                lora(4)

            flag1 = pe.alloc_register("delta1_bits")
            pe.wait_ge(s_id, 8 + E)
            pe.reg_load(flag1, V["dl1"][0:1, :].bitcast(I32))
            transposes(0)
            with pe.If_ne(flag1, 0):
                stage1(True)
            with pe.Else():
                stage1(False)

            LATE = 11
            pe.wait_ge(s_ye, 4)
            pe.wait_ge(s_epi, NCH * TILES)
            for kt in range(LATE):
                pe.wait_ge(s_lo, kt + 1)
                for c in range(5):
                    products(c, [kt], 0, kt == 0)
            pe.wait_ge(s_lo, KT)
            for c in range(5):
                products(c, range(LATE, KT), 0, False).then_inc(s_m2, 1)
                if c == 1:
                    y_transposes(1, 0)
                    y_transposes(1, 1)
                if c == 3:
                    y_transposes(1, 2)
                    y_transposes(1, 3)
            z_transposes(0)
            pe.wait_ge(s_ze, 1)
            pe.wait_ge(s_bback, 16)
            for c in range(5):
                lora(c)
            with pe.Fori(0, TILES // 2 - 1) as i2:
                for o in range(2):
                    tile2(i2 * 2 + (1 + o), 1 - o, True)
            tile2(TILES - 1, 1, False)


def kernel(x, ctx_4096, g_xattn, g_ffn, L0_xattn_x1_scale, L0_xattn_x1_zp, L0_xattn_x2_scale, L0_xattn_x2_zp,
           L0_ffn_W_up, L0_ffn_gate_w, L0_ffn_expert_bias, L0_ffn_lora_A, L0_ffn_lora_B):
    import numpy as np
    import concourse.bacc as bacc
    from concourse.bass_utils import run_bass_kernel_spmd

    a = lambda v: np.asarray(v)
    B, S, D = x.shape
    E, R = L0_ffn_lora_A.shape[:2]
    arrays = {
        "x": a(x).reshape(B * S, D),
        "ctx": a(ctx_4096).reshape(-1, D),
        "w": np.ascontiguousarray(np.concatenate(
            [a(L0_ffn_gate_w), a(L0_ffn_lora_A).reshape(E * R, D), a(L0_ffn_W_up)], axis=0).T),
        "b_t": np.ascontiguousarray(a(L0_ffn_lora_B).transpose(0, 2, 1).reshape(E * R, D)),
        "scal": np.ascontiguousarray(np.tile(np.concatenate([a(v).reshape(-1) for v in (
            L0_xattn_x1_scale, L0_xattn_x1_zp, L0_xattn_x2_scale, L0_xattn_x2_zp, g_xattn, g_ffn,
            L0_ffn_expert_bias)])[None, :], (P, 1))),
    }
    nc = bacc.Bacc("TRN2", target_bir_lowering=False, num_devices=1)
    aps = {n: nc.dram_tensor(f"in_{n}", v.shape, mybir.dt.from_np(v.dtype), kind="ExternalInput").ap()
           for n, v in arrays.items()}
    out = nc.dram_tensor("out_0", (B * S, D), F32, kind="ExternalOutput").ap()
    build(nc, **aps, out=out)
    r = run_bass_kernel_spmd(nc, [{f"in_{n}": v for n, v in arrays.items()}], core_ids=[0])
    return r.results[0]["out_0"].reshape(B, S, D)
```
